# Optimizing a Trainium2 kernel written in Bass

```python
import numpy as np
import jax
import jax.numpy as jnp

def _softmax(x, axis=-1):
    return jax.nn.softmax(x, axis=axis)

def _gelu(x):
    return jax.nn.gelu(x, approximate=True)

def _silu(x):
    return jax.nn.silu(x)

def _sigmoid(x):
    return jax.nn.sigmoid(x)

def _layernorm(x, axis=-1, eps=1e-05):
    m = jnp.mean(x, axis=axis, keepdims=True)
    v = jnp.var(x, axis=axis, keepdims=True)
    return (x - m) / jnp.sqrt(v + eps)

def _scatter_add(tgt, idx, src, axis=0):
    return tgt.at[idx].add(src)

def _segment_sum(src, seg, n):
    return jax.ops.segment_sum(src, seg, n)
kernel_name = 'mk_dlrm_tower_d1_rec_r8_28fd13'

def setup_inputs(seed: int=0):
    np.random.seed(seed)
    _w = jnp.asarray

    def _rec_inputs():
        import jax
        import jax.numpy as jnp
        _tk = jax.random.key(seed)
        ids = jnp.stack([jax.random.randint(jax.random.fold_in(_tk, 200 + f), (2048,), 0, v, jnp.int32) for f, v in enumerate([12500, 1250, 1000, 125000, 1250, 12500, 12500, 12500, 12500, 1250, 12500, 1250, 12500, 1250, 12500, 1250, 1000, 1000, 1000, 1250, 1250, 1250, 1250, 1250, 1000, 1000])], axis=1)
        tbl_0 = 0.05 * jax.random.normal(jax.random.fold_in(_tk, 500 + 0), (12500, 128), jnp.float32)
        tbl_1 = 0.05 * jax.random.normal(jax.random.fold_in(_tk, 500 + 1), (1250, 128), jnp.float32)
        tbl_2 = 0.05 * jax.random.normal(jax.random.fold_in(_tk, 500 + 2), (1000, 128), jnp.float32)
        tbl_3 = 0.05 * jax.random.normal(jax.random.fold_in(_tk, 500 + 3), (125000, 128), jnp.float32)
        tbl_4 = 0.05 * jax.random.normal(jax.random.fold_in(_tk, 500 + 4), (1250, 128), jnp.float32)
        tbl_5 = 0.05 * jax.random.normal(jax.random.fold_in(_tk, 500 + 5), (12500, 128), jnp.float32)
        tbl_6 = 0.05 * jax.random.normal(jax.random.fold_in(_tk, 500 + 6), (12500, 128), jnp.float32)
        tbl_7 = 0.05 * jax.random.normal(jax.random.fold_in(_tk, 500 + 7), (12500, 128), jnp.float32)
        tbl_8 = 0.05 * jax.random.normal(jax.random.fold_in(_tk, 500 + 8), (12500, 128), jnp.float32)
        tbl_9 = 0.05 * jax.random.normal(jax.random.fold_in(_tk, 500 + 9), (1250, 128), jnp.float32)
        tbl_10 = 0.05 * jax.random.normal(jax.random.fold_in(_tk, 500 + 10), (12500, 128), jnp.float32)
        tbl_11 = 0.05 * jax.random.normal(jax.random.fold_in(_tk, 500 + 11), (1250, 128), jnp.float32)
        tbl_12 = 0.05 * jax.random.normal(jax.random.fold_in(_tk, 500 + 12), (12500, 128), jnp.float32)
        tbl_13 = 0.05 * jax.random.normal(jax.random.fold_in(_tk, 500 + 13), (1250, 128), jnp.float32)
        tbl_14 = 0.05 * jax.random.normal(jax.random.fold_in(_tk, 500 + 14), (12500, 128), jnp.float32)
        tbl_15 = 0.05 * jax.random.normal(jax.random.fold_in(_tk, 500 + 15), (1250, 128), jnp.float32)
        tbl_16 = 0.05 * jax.random.normal(jax.random.fold_in(_tk, 500 + 16), (1000, 128), jnp.float32)
        tbl_17 = 0.05 * jax.random.normal(jax.random.fold_in(_tk, 500 + 17), (1000, 128), jnp.float32)
        tbl_18 = 0.05 * jax.random.normal(jax.random.fold_in(_tk, 500 + 18), (1000, 128), jnp.float32)
        tbl_19 = 0.05 * jax.random.normal(jax.random.fold_in(_tk, 500 + 19), (1250, 128), jnp.float32)
        tbl_20 = 0.05 * jax.random.normal(jax.random.fold_in(_tk, 500 + 20), (1250, 128), jnp.float32)
        tbl_21 = 0.05 * jax.random.normal(jax.random.fold_in(_tk, 500 + 21), (1250, 128), jnp.float32)
        tbl_22 = 0.05 * jax.random.normal(jax.random.fold_in(_tk, 500 + 22), (1250, 128), jnp.float32)
        tbl_23 = 0.05 * jax.random.normal(jax.random.fold_in(_tk, 500 + 23), (1250, 128), jnp.float32)
        tbl_24 = 0.05 * jax.random.normal(jax.random.fold_in(_tk, 500 + 24), (1000, 128), jnp.float32)
        tbl_25 = 0.05 * jax.random.normal(jax.random.fold_in(_tk, 500 + 25), (1000, 128), jnp.float32)
        _rk = jax.random.fold_in(_tk, 7)
        r_dense_output = -0.000520686 + 1.00062 * jax.random.normal(jax.random.fold_in(_rk, 101), (2048, 128), jnp.float32)
        W_top1 = 0.0405887 * jax.random.normal(jax.random.fold_in(_tk, 801), (607, 512), jnp.float32)
        W_top2 = 0.0441942 * jax.random.normal(jax.random.fold_in(_tk, 802), (512, 256), jnp.float32)
        W_top3 = 0.0625 * jax.random.normal(jax.random.fold_in(_tk, 803), (256, 1), jnp.float32)
        b_top1 = jnp.zeros((512,), jnp.float32)
        b_top2 = jnp.zeros((256,), jnp.float32)
        return (r_dense_output, ids, tbl_0, tbl_1, tbl_2, tbl_3, tbl_4, tbl_5, tbl_6, tbl_7, tbl_8, tbl_9, tbl_10, tbl_11, tbl_12, tbl_13, tbl_14, tbl_15, tbl_16, tbl_17, tbl_18, tbl_19, tbl_20, tbl_21, tbl_22, tbl_23, tbl_24, tbl_25, W_top1, b_top1, W_top2, b_top2, W_top3)
    r_dense_output, ids, tbl_0, tbl_1, tbl_2, tbl_3, tbl_4, tbl_5, tbl_6, tbl_7, tbl_8, tbl_9, tbl_10, tbl_11, tbl_12, tbl_13, tbl_14, tbl_15, tbl_16, tbl_17, tbl_18, tbl_19, tbl_20, tbl_21, tbl_22, tbl_23, tbl_24, tbl_25, W_top1, b_top1, W_top2, b_top2, W_top3 = _rec_inputs()

    def _L0_rec_setup():
        import jax, jax.numpy as jnp
        import numpy as np
        B, NUM_SPARSE, D = (2048, 26, 128)
        key = jax.random.key(seed)
        k1, k2 = jax.random.split(key)
        dense_output = jax.random.normal(k1, (B, D), dtype=jnp.float32)
        embeddings = jax.random.normal(k2, (B, NUM_SPARSE, D), dtype=jnp.float32)
        return {'dense_output': dense_output, 'embeddings': embeddings}
    _L0_rec_all = _L0_rec_setup()
    _L0_rec_in = {k: v for k, v in _L0_rec_all.items() if k in ()}
    del _L0_rec_all
    return {'r_dense_output': r_dense_output, 'ids': ids, 'tbl_0': tbl_0, 'tbl_1': tbl_1, 'tbl_2': tbl_2, 'tbl_3': tbl_3, 'tbl_4': tbl_4, 'tbl_5': tbl_5, 'tbl_6': tbl_6, 'tbl_7': tbl_7, 'tbl_8': tbl_8, 'tbl_9': tbl_9, 'tbl_10': tbl_10, 'tbl_11': tbl_11, 'tbl_12': tbl_12, 'tbl_13': tbl_13, 'tbl_14': tbl_14, 'tbl_15': tbl_15, 'tbl_16': tbl_16, 'tbl_17': tbl_17, 'tbl_18': tbl_18, 'tbl_19': tbl_19, 'tbl_20': tbl_20, 'tbl_21': tbl_21, 'tbl_22': tbl_22, 'tbl_23': tbl_23, 'tbl_24': tbl_24, 'tbl_25': tbl_25, 'W_top1': W_top1, 'b_top1': b_top1, 'W_top2': W_top2, 'b_top2': b_top2, 'W_top3': W_top3}

def reference(r_dense_output, ids, tbl_0, tbl_1, tbl_2, tbl_3, tbl_4, tbl_5, tbl_6, tbl_7, tbl_8, tbl_9, tbl_10, tbl_11, tbl_12, tbl_13, tbl_14, tbl_15, tbl_16, tbl_17, tbl_18, tbl_19, tbl_20, tbl_21, tbl_22, tbl_23, tbl_24, tbl_25, W_top1, b_top1, W_top2, b_top2, W_top3):
    import jax
    import jax.numpy as jnp

    def _L0_rec_ref(dense_output, embeddings):
        import jax, jax.numpy as jnp
        import numpy as np
        B, NUM_SPARSE, D = (2048, 26, 128)
        combined = jnp.concatenate([dense_output[:, None, :], embeddings], axis=1)
        interactions = jnp.einsum('bfd,bgd->bfg', combined, combined)
        F = combined.shape[1]
        iu, ju = jnp.triu_indices(F, k=1)
        interactions_flat = interactions[:, iu, ju]
        return jnp.concatenate([dense_output, interactions_flat], axis=1)
    e = jnp.stack([tbl_0[ids[:, 0]], tbl_1[ids[:, 1]], tbl_2[ids[:, 2]], tbl_3[ids[:, 3]], tbl_4[ids[:, 4]], tbl_5[ids[:, 5]], tbl_6[ids[:, 6]], tbl_7[ids[:, 7]], tbl_8[ids[:, 8]], tbl_9[ids[:, 9]], tbl_10[ids[:, 10]], tbl_11[ids[:, 11]], tbl_12[ids[:, 12]], tbl_13[ids[:, 13]], tbl_14[ids[:, 14]], tbl_15[ids[:, 15]], tbl_16[ids[:, 16]], tbl_17[ids[:, 17]], tbl_18[ids[:, 18]], tbl_19[ids[:, 19]], tbl_20[ids[:, 20]], tbl_21[ids[:, 21]], tbl_22[ids[:, 22]], tbl_23[ids[:, 23]], tbl_24[ids[:, 24]], tbl_25[ids[:, 25]]], axis=1)
    z = _L0_rec_ref(r_dense_output, e)
    z = z.reshape(z.shape[0], -1)
    h = jnp.concatenate([z, r_dense_output], axis=1)
    h = jnp.maximum(h @ W_top1 + b_top1, 0.0)
    h = jnp.maximum(h @ W_top2 + b_top2, 0.0)
    y = h @ W_top3
    return y

_drawn_inputs = setup_inputs


def setup_inputs(seed=0):
    import zlib

    import numpy as np

    out = dict(_drawn_inputs(seed))
    spreads = {'b_top1': (0.0, 0.1), 'b_top2': (0.0, 0.1)}
    factors = {}
    for name, (base, spread) in spreads.items():
        noise = np.random.default_rng([zlib.crc32(name.encode()), seed]).standard_normal(out[name].shape)
        drawn = base * np.exp(spread * noise) if base else spread * noise
        out[name] = jnp.asarray(drawn.astype(out[name].dtype))
    for name, factor in factors.items():
        out[name] = (out[name] * factor).astype(out[name].dtype)
    return out
```

```python
from contextlib import ExitStack

import concourse.bass as bass
from concourse import mybir

BATCH, FIELDS, D = 2048, 26, 128
ROWS_1000 = 1000
ONEHOT_FIELDS = (2, 16, 17, 18, 24, 25)
GATHER_FIELDS = tuple(f for f in range(FIELDS) if f not in ONEHOT_FIELDS)
K1H, NGATHER = len(ONEHOT_FIELDS), len(GATHER_FIELDS)
FEATURES = FIELDS + 1
SLOT_PITCH = 32
TILE, PAIR = 128, 256
PAIRS = BATCH // PAIR
J = 4
GROUPS = TILE // J
GRP = 4
NGRP = NGATHER // GRP
KT, KROWS = 8, ROWS_1000 // 8
NEIGHBOURS = FEATURES - 1
GRAM_COLS = J * NEIGHBOURS
GRAMS_PER_BANK = 4
GBANKS = GROUPS // GRAMS_PER_BANK
H1, H2 = 512, 256
M1, M2 = H1 // 128, H2 // 128

COLUMN_GROUPS = [(g - 2, g) for g in range(NEIGHBOURS, 2, -3)] + [(1, 2)]
RTILES = 3
ZROWS = sum(last for _, last in COLUMN_GROUPS)
SHIFTS = len(COLUMN_GROUPS)


def build(nc, ids_gather, ids_onehot, dense_t, tables, identity, select, row_index,
          w_pairs, w_dense, b1, w2, b2, w3, y_out):
    f32, f32r, f16, i32 = mybir.dt.float32, mybir.dt.float32r, mybir.dt.float16, mybir.dt.int32
    ALU, ACT = mybir.AluOpType, mybir.ActivationFunctionType

    with ExitStack() as ctx:
        def sbuf(name, shape, dt):
            return ctx.enter_context(nc.sbuf_tensor(name, shape, dt))

        def sem(name):
            return ctx.enter_context(nc.semaphore(name))

        index = [sbuf(f"index{u}", [128, NGATHER], i32) for u in range(2)]
        rows = [sbuf(f"rows{u}", [128, NGATHER, D], f32) for u in range(2)]
        features = sbuf("features", [128, 2, TILE, SLOT_PITCH], f32)
        blocks = sbuf("blocks", [128, J, NEIGHBOURS, PAIR // J], f32)
        z = sbuf("z", [128, J, RTILES, PAIR // J], f32)
        dense = sbuf("dense", [128, BATCH], f32)
        table_hi = sbuf("table_hi", [128, K1H, KT, D], f32r)
        table_lo = sbuf("table_lo", [128, K1H, KT, D], f32r)
        onehot = sbuf("onehot", [128, 3, KT, PAIR], f32r)
        ids16 = sbuf("ids16", [128, BATCH], f16)
        sel = sbuf("sel", [128, K1H, KROWS], f16)
        row_idx = sbuf("row_idx", [128, KT], f32)
        ident = sbuf("ident", [128, 128], f32)
        w1z = sbuf("w1z", [128, RTILES, H1], f32)
        w1ab = sbuf("w1ab", [128, 2, H1], f32)
        w1d = sbuf("w1d", [128, H1], f32)
        w2s = sbuf("w2s", [128, M1, H2], f32)
        w3s = sbuf("w3s", [128, M2], f32)
        b1s = sbuf("b1s", [128, M1], f32)
        b2s = sbuf("b2s", [128, M2], f32)
        hidden1 = sbuf("hidden1", [128, M1, PAIR], f32)
        hidden2 = sbuf("hidden2", [128, M2, PAIR], f32)
        ids_and_y = sbuf("ids_and_y", [128, BATCH], i32)
        ids_raw = ids_and_y[0:K1H, :]
        y_row = ids_and_y[0:1, :].bitcast(f32)
        table_raw = blocks[:, :, :, :].rearrange("p j g c -> p (j g c)")[:, 0:K1H * KT * D].rearrange(
            "p (k t d) -> p k t d", k=K1H, t=KT)

        t_bank = [ctx.enter_context(nc.psum_tensor(f"t_bank{i}", [128, GRP, TILE], f32)) for i in range(2)]
        g_bank = [ctx.enter_context(nc.psum_tensor(f"g_bank{i}", [128, 512], f32)) for i in range(2)]
        ids_bank = ctx.enter_context(nc.psum_tensor("ids_bank", [128, 2, PAIR], f32))
        x_bank = [ctx.enter_context(nc.psum_tensor(f"x_bank{i}", [128, 512], f32)) for i in range(2)]

        index_loaded = [sem(f"index_loaded{u}") for u in range(2)]
        gathered = [[sem(f"gathered{u}_{g}") for g in range(NGRP)] for u in range(2)]
        gather_begun = sem("gather_begun")
        onehot_ids_loaded = sem("onehot_ids_loaded")
        sel_loaded = sem("sel_loaded")
        row_idx_loaded = sem("row_idx_loaded")
        ident_loaded = sem("ident_loaded")
        dense_loaded = sem("dense_loaded")
        table_loaded = [sem(f"table_loaded{k}") for k in range(K1H)]
        w1z_loaded = sem("w1z_loaded")
        w1ab_loaded = sem("w1ab_loaded")
        tail_weights_loaded = sem("tail_weights_loaded")
        cleared = sem("cleared")
        ids16_ready = sem("ids16_ready")
        w1d_ready = sem("w1d_ready")
        table_hi_ready = sem("table_hi_ready")
        table_split = sem("table_split")
        ids_spread = sem("ids_spread")
        onehot_made = sem("onehot_made")
        lookup_done = sem("lookup_done")
        lookup_copied = sem("lookup_copied")
        dense_placed = sem("dense_placed")
        transposed = sem("transposed")
        transpose_copied = sem("transpose_copied")
        gram_done = sem("gram_done")
        gram_copied = sem("gram_copied")
        z_shifted = sem("z_shifted")
        h1_summed = sem("h1_summed")
        h1_ready = sem("h1_ready")
        h2_summed = sem("h2_summed")
        h2_ready = sem("h2_ready")
        y_summed = sem("y_summed")
        y_copied = sem("y_copied")
        y_stored = sem("y_stored")

        block = ctx.enter_context(nc.Block())

        def over_pairs(eng, step):
            step(0, True, False)
            with eng.Fori(1, PAIRS - 1) as s:
                step(s, False, False)
            step(PAIRS - 1, False, True)

        @block.sync
        def _(sp):
            def load_index(tile, u):
                sp.dma_start(index[u][:, :], ids_gather[bass.ds(tile, 1), :, :]
                             .rearrange("a p f -> (a p) f")).then_inc(index_loaded[u], 16)

            def value(x):
                return x if isinstance(x, int) else sp.snap(x)

            load_index(0, 0)
            load_index(1, 1)
            sp.dma_start(ids_raw, ids_onehot).then_inc(onehot_ids_loaded, 16)
            sp.dma_start(sel[:, :, :], select).then_inc(sel_loaded, 16)
            sp.dma_start(row_idx[0:KROWS, :], row_index).then_inc(row_idx_loaded, 16)
            for k in range(K1H):
                sp.dma_start(table_raw[0:KROWS, k, :, :],
                             tables[ONEHOT_FIELDS[k]].rearrange("(p t) d -> p t d", t=KT)
                             ).then_inc(table_loaded[k], 16)
            sp.dma_start(ident[:, :], identity).then_inc(ident_loaded, 16)
            sp.dma_start(dense[:, :], dense_t).then_inc(dense_loaded, 16)
            sp.dma_start(w1z[0:ZROWS, :, :], w_pairs).then_inc(w1z_loaded, 16)
            sp.dma_start(w1ab[:, :, :], w_dense.rearrange("a p n -> p a n")).then_inc(w1ab_loaded, 16)
            sp.dma_start(w2s[:, :, :], w2.rearrange("(k p) n -> p k n", p=128)).then_inc(tail_weights_loaded, 16)
            sp.dma_start(w3s[:, :], w3).then_inc(tail_weights_loaded, 16)
            sp.dma_start(b1s[:, :], b1).then_inc(tail_weights_loaded, 16)
            sp.dma_start(b2s[:, :], b2).then_inc(tail_weights_loaded, 16)

            def step(s, first, last):
                landed = value(16 * GRP * (s + 1))
                next_tile = [value(2 * s + 2 + u) for u in range(2)]
                copied = value(2 * GBANKS * (s + 1))
                for u in range(2):
                    if not last:
                        for g in range(NGRP):
                            sp.wait_ge(gathered[u][g], landed)
                        load_index(next_tile[u], u)
                sp.wait_ge(gram_copied, copied)
                base = 0
                for lo, hi in COLUMN_GROUPS:
                    n = hi - lo + 1
                    sp.dma_start(z[base:base + hi, :, 0:n, :], blocks[0:hi, :, lo - 1:hi, :]
                                 ).then_inc(z_shifted, 16)
                    base += hi

            over_pairs(sp, step)
            sp.wait_ge(y_copied, PAIRS)
            sp.dma_start(y_out.rearrange("(a n) o -> a (n o)", a=1), y_row).then_inc(y_stored, 16)
            sp.wait_ge(y_stored, 16)

        @block.gpsimd
        def _(pool):
            def step(s, first, last):
                for u in range(2):
                    pool.wait_ge(index_loaded[u], 16 * (s + 1))
                    if not first:
                        pool.wait_ge(transposed, 2 * NGRP * s - NGRP * (1 - u))
                    pool.sem_inc(gather_begun, 1)
                    for n, f in enumerate(GATHER_FIELDS):
                        pool.indirect_dma_start(
                            out=rows[u][:, n, :], out_offset=None, in_=tables[f],
                            in_offset=bass.IndirectOffsetOnAxis(ap=index[u][:, n:n + 1], axis=0)
                        ).then_inc(gathered[u][n // GRP], 16)

            over_pairs(pool, step)

        @block.vector
        def _(dve):
            dve.memset(ids16[:, :], 0.0).then_inc(cleared, 1)
            dve.memset(z[:, :, :, :], 0.0).then_inc(cleared, 1)
            dve.memset(features[:, :, :, FEATURES:SLOT_PITCH], 0.0).then_inc(cleared, 1)
            dve.wait_ge(onehot_ids_loaded, 16)
            dve.wait_ge(cleared, 1)
            dve.tensor_copy(ids16[0:K1H, :], ids_raw).then_inc(ids16_ready, 1)
            for k in range(K1H):
                dve.wait_ge(table_hi_ready, k + 1)
                dve.tensor_tensor(table_lo[0:KROWS, k, :, :], table_raw[0:KROWS, k, :, :],
                                  table_hi[0:KROWS, k, :, :].bitcast(f32), ALU.subtract).then_inc(table_split, 1)
            dve.wait_ge(w1ab_loaded, 16)
            dve.tensor_tensor(w1d[:, :], w1ab[:, 0, :], w1ab[:, 1, :], ALU.add).then_inc(w1d_ready, 1)
            dve.wait_ge(row_idx_loaded, 16)

            def make_onehot(s, k, first):
                dve.wait_ge(ids_spread, (K1H // 2) * s + k // 2 + 1)
                if not (first and k < 3):
                    dve.wait_ge(lookup_done, K1H * s + k - 2)
                dve.tensor_tensor(
                    onehot[0:KROWS, k % 3, :, :],
                    ids_bank[0:KROWS, k % 2, :].unsqueeze(1).broadcast_to([KROWS, KT, PAIR]),
                    row_idx[0:KROWS, :].unsqueeze(2).broadcast_to([KROWS, KT, PAIR]),
                    ALU.is_equal).then_inc(onehot_made, 1)

            def copy_blocks(s, u, first):
                if u == 0 and not first:
                    dve.wait_ge(z_shifted, 16 * SHIFTS * s)
                for i in range(GBANKS):
                    dve.wait_ge(gram_done, 2 * GBANKS * s + GBANKS * u + i + 1)
                    bank = g_bank[i % 2][:, 0:GRAMS_PER_BANK * GRAM_COLS].rearrange(
                        "p (t j g) -> p j g t", t=GRAMS_PER_BANK, j=J)
                    col = GROUPS * u + GRAMS_PER_BANK * i
                    for j in range(J):
                        last_copy = dve.tensor_copy(
                            blocks[0:NEIGHBOURS, j, :, col:col + GRAMS_PER_BANK],
                            bank[SLOT_PITCH * j:SLOT_PITCH * j + NEIGHBOURS, j, :, :])
                    last_copy.then_inc(gram_copied, 1)

            def step(s, first, last):
                for k in range(2, K1H):
                    make_onehot(s, k, first)
                copy_blocks(s, 0, first)
                if not last:
                    for k in range(2):
                        make_onehot(s + 1, k, False)
                copy_blocks(s, 1, first)

            for k in range(2):
                make_onehot(0, k, True)
            over_pairs(dve, step)

        @block.scalar
        def _(act):
            for k in range(K1H):
                act.wait_ge(table_loaded[k], 16)
                act.activation(table_hi[0:KROWS, k, :, :], table_raw[0:KROWS, k, :, :],
                               ACT.Copy).then_inc(table_hi_ready, 1)
            act.wait_ge(dense_loaded, 16)
            act.wait_ge(tail_weights_loaded, 64)

            def slot(i):
                return features[:, :, :, i].rearrange("d u (t j) -> d j u t", j=J)

            def in_order(cols):
                return cols.rearrange("d (j u t) -> d j u t", j=J, u=2)

            def copy_transposes(s, u):
                for g in range(NGRP):
                    act.wait_ge(transposed, NGRP * (2 * s + u) + g + 1)
                    act.activation(features[:, u, :, 1 + GRP * g:1 + GRP * (g + 1)],
                                   t_bank[(NGRP * u + g) % 2][:, :, :].rearrange("d f p -> d p f"),
                                   ACT.Copy).then_inc(transpose_copied, 1)

            def relu1(s):
                for m in range(M1):
                    act.wait_ge(h1_summed, M1 * s + m + 1)
                    act.activation(hidden1[:, m, :], x_bank[m % 2][:, 0:PAIR], ACT.Relu,
                                   bias=b1s[:, m:m + 1]).then_inc(h1_ready, 1)

            def relu2_and_y(s):
                for m in range(M2):
                    act.wait_ge(h2_summed, M2 * s + m + 1)
                    act.activation(hidden2[:, m, :], x_bank[m][:, 0:PAIR], ACT.Relu,
                                   bias=b2s[:, m:m + 1]).then_inc(h2_ready, 1)
                act.wait_ge(y_summed, s + 1)
                act.activation(y_row[:, bass.ds(s * PAIR, PAIR)], x_bank[0][0:1, 0:PAIR],
                               ACT.Copy).then_inc(y_copied, 1)

            def step(s, first, last):
                if not first:
                    act.wait_ge(gram_done, 2 * GBANKS * s)
                act.activation(slot(0), in_order(dense[:, bass.ds(s * PAIR, PAIR)]),
                               ACT.Copy).then_inc(dense_placed, 1)
                for k in range(K1H):
                    act.wait_ge(lookup_done, K1H * s + k + 1)
                    act.activation(slot(1 + NGATHER + k), in_order(x_bank[k % 2][:, 0:PAIR]),
                                   ACT.Copy).then_inc(lookup_copied, 1)
                copy_transposes(s, 0)
                if not first:
                    relu1(s - 1)
                copy_transposes(s, 1)
                if not first:
                    relu2_and_y(s - 1)

            over_pairs(act, step)
            relu1(PAIRS - 1)
            relu2_and_y(PAIRS - 1)

        @block.tensor
        def _(pe):
            def spread_ids(s, q, first):
                if not (first and q == 0):
                    pe.wait_ge(onehot_made, K1H * s + 2 * q)
                for i in range(2):
                    last_mm = pe.matmul(ids_bank[0:KROWS, i, :], sel[:, 2 * q + i, :],
                                        ids16[:, bass.ds(s * PAIR, PAIR)], start=True, stop=True)
                last_mm.then_inc(ids_spread, 1)

            def look_up(s, k, first):
                pe.wait_ge(onehot_made, K1H * s + k + 1)
                if first:
                    pe.wait_ge(table_split, k + 1)
                if not (first and k < 2):
                    pe.wait_ge(lookup_copied, K1H * s + k - 1)
                for kt in range(KT):
                    for part, table in enumerate((table_hi, table_lo)):
                        last_mm = pe.matmul(x_bank[k % 2][:, 0:PAIR], table[0:KROWS, k, kt, :],
                                            onehot[0:KROWS, k % 3, kt, :],
                                            start=kt + part == 0, stop=kt + part == KT)
                last_mm.then_inc(lookup_done, 1)

            def transpose_rows(s, u, first):
                for g in range(NGRP):
                    n = NGRP * u + g
                    pe.wait_ge(gathered[u][g], 16 * GRP * (s + 1))
                    if not (first and n < 2):
                        pe.wait_ge(transpose_copied, 2 * NGRP * s + n - 1)
                    for i in range(GRP):
                        last_mm = pe.transpose(t_bank[n % 2][:, i, :], rows[u][:, GRP * g + i, :], ident[:, :])
                    last_mm.then_inc(transposed, 1)

            def multiply_features(s, u, first):
                pe.wait_ge(transpose_copied, NGRP * (2 * s + u + 1))
                pe.wait_ge(lookup_copied, K1H * (s + 1))
                pe.wait_ge(dense_placed, s + 1)
                for i in range(GBANKS):
                    n = GBANKS * u + i
                    if not (first and n < 2):
                        pe.wait_ge(gram_copied, 2 * GBANKS * s + n - 1)
                    for t in range(GRAMS_PER_BANK):
                        p = J * (GRAMS_PER_BANK * i + t)
                        last_mm = pe.matmul(
                            g_bank[i % 2][:, GRAM_COLS * t:GRAM_COLS * (t + 1)],
                            features[:, u, p:p + J, :].rearrange("d j f -> d (j f)"),
                            features[:, u, p:p + J, 1:FEATURES], start=True, stop=True)
                    last_mm.then_inc(gram_done, 1)

            def layer1(s, last):
                pe.wait_ge(z_shifted, 16 * SHIFTS * (s + 1))
                if last:
                    pe.wait_ge(h2_ready, M2 * s)
                    pe.wait_ge(y_copied, s)
                for m in range(M1):
                    if m >= 2:
                        pe.wait_ge(h1_ready, M1 * s + m - 1)
                    cols = slice(128 * m, 128 * (m + 1))
                    pe.matmul(x_bank[m % 2][:, 0:PAIR], w1d[:, cols], dense[:, bass.ds(s * PAIR, PAIR)],
                              start=True, stop=False)
                    for r in range(RTILES):
                        last_mm = pe.matmul(x_bank[m % 2][:, 0:PAIR], w1z[0:ZROWS, r, cols],
                                            z[0:ZROWS, :, r, :], start=False, stop=r == RTILES - 1)
                    last_mm.then_inc(h1_summed, 1)

            def layer2(s):
                pe.wait_ge(h1_ready, M1 * (s + 1))
                for m in range(M2):
                    for k in range(M1):
                        last_mm = pe.matmul(x_bank[m][:, 0:PAIR], w2s[:, k, 128 * m:128 * (m + 1)],
                                            hidden1[:, k, :], start=k == 0, stop=k == M1 - 1)
                    last_mm.then_inc(h2_summed, 1)

            def layer3(s):
                pe.wait_ge(h2_ready, M2 * (s + 1))
                for k in range(M2):
                    last_mm = pe.matmul(x_bank[0][0:1, 0:PAIR], w3s[:, k:k + 1], hidden2[:, k, :],
                                        start=k == 0, stop=k == M2 - 1)
                last_mm.then_inc(y_summed, 1)

            def step(s, first, last):
                spread_ids(s, 1, first)
                if not first:
                    pe.wait_ge(dense_placed, s + 1)
                look_up(s, 0, first)
                look_up(s, 1, first)
                spread_ids(s, 2, first)
                for k in range(2, K1H):
                    look_up(s, k, first)
                if first:
                    pe.wait_ge(ident_loaded, 16)
                transpose_rows(s, 0, first)
                multiply_features(s, 0, first)
                if not last:
                    spread_ids(s + 1, 0, False)
                if not first:
                    layer1(s - 1, False)
                transpose_rows(s, 1, first)
                if not first:
                    layer2(s - 1)
                multiply_features(s, 1, first)
                if not first:
                    layer3(s - 1)

            pe.wait_ge(sel_loaded, 16)
            pe.wait_ge(ids16_ready, 1)
            pe.wait_ge(cleared, 3)
            spread_ids(0, 0, True)
            pe.wait_ge(w1z_loaded, 16)
            pe.wait_ge(w1d_ready, 1)
            pe.wait_ge(tail_weights_loaded, 64)
            over_pairs(pe, step)
            layer1(PAIRS - 1, True)
            layer2(PAIRS - 1)
            layer3(PAIRS - 1)


def pair_weight_rows():
    feature = (0,) + tuple(f + 1 for f in GATHER_FIELDS) + tuple(f + 1 for f in ONEHOT_FIELDS)
    at = []
    for lo, hi in COLUMN_GROUPS:
        for left in range(hi):
            line = []
            for right in range(lo, lo + RTILES):
                if left < right <= hi:
                    a, b = sorted((feature[left], feature[right]))
                    line.append(D + a * (2 * FEATURES - a - 1) // 2 + b - a - 1)
                else:
                    line.append(-1)
            at.append(line)
    return at


def kernel(**inputs):
    import numpy as np
    import concourse.bacc as bacc
    from concourse.bass_utils import run_bass_kernel_spmd

    ids = np.asarray(inputs["ids"])
    w1 = np.asarray(inputs["W_top1"])
    at = np.array(pair_weight_rows())
    w_pairs = np.zeros((ZROWS, RTILES, H1), w1.dtype)
    w_pairs[at >= 0] = w1[at[at >= 0]]
    select = np.zeros((128, K1H, KROWS), np.float16)
    for k in range(K1H):
        select[k, k, :] = 1.0
    by_tile = ids.reshape(PAIRS, J, 2, GROUPS, FIELDS).transpose(0, 2, 3, 1, 4)
    arrays = {
        "ids_gather": by_tile[..., list(GATHER_FIELDS)].reshape(2 * PAIRS, TILE, NGATHER),
        "ids_onehot": ids[:, list(ONEHOT_FIELDS)].T,
        "dense_t": np.asarray(inputs["r_dense_output"]).T,
        "identity": np.eye(128, dtype=np.float32),
        "select": select,
        "row_index": np.arange(ROWS_1000, dtype=np.float32).reshape(KROWS, KT),
        "w_pairs": w_pairs,
        "w_dense": np.stack([w1[:D], w1[-D:]]),
        "b1": np.asarray(inputs["b_top1"]).reshape(M1, 128).T,
        "w2": np.asarray(inputs["W_top2"]),
        "b2": np.asarray(inputs["b_top2"]).reshape(M2, 128).T,
        "w3": np.asarray(inputs["W_top3"]).reshape(M2, 128).T,
    }
    arrays |= {f"tbl_{f}": np.asarray(inputs[f"tbl_{f}"]) for f in range(FIELDS)}
    arrays = {name: np.ascontiguousarray(a) for name, a in arrays.items()}

    nc = bacc.Bacc("TRN2", target_bir_lowering=False, num_devices=1)
    ap = {name: nc.dram_tensor(name, a.shape, mybir.dt.from_np(a.dtype), kind="ExternalInput").ap()
          for name, a in arrays.items()}
    y = nc.dram_tensor("y", (BATCH, 1), mybir.dt.float32, kind="ExternalOutput").ap()
    build(nc, ap["ids_gather"], ap["ids_onehot"], ap["dense_t"], [ap[f"tbl_{f}"] for f in range(FIELDS)],
          ap["identity"], ap["select"], ap["row_index"], ap["w_pairs"], ap["w_dense"], ap["b1"], ap["w2"],
          ap["b2"], ap["w3"], y)
    return run_bass_kernel_spmd(nc, [arrays], core_ids=[0]).results[0]["y"]
```

```python
from contextlib import ExitStack

import concourse.bass as bass
from concourse import mybir

BATCH, FIELDS, D = 2048, 26, 128
ROWS_1000 = 1000
LOOKUP_BANK = (0, 1, 0, 0, 1, 0)
ONEHOT_FIELDS = (2, 16, 17, 18, 24, 25)
GATHER_FIELDS = tuple(f for f in range(FIELDS) if f not in ONEHOT_FIELDS)
K1H, NGATHER = len(ONEHOT_FIELDS), len(GATHER_FIELDS)
FEATURES = FIELDS + 1
SLOT_PITCH = 32
TILE, PAIR = 128, 256
PAIRS = BATCH // PAIR
J = 4
GROUPS = TILE // J
GRP = 4
NGRP = NGATHER // GRP
KT, KROWS = 8, ROWS_1000 // 8
NEIGHBOURS = FEATURES - 1
GRAM_COLS = J * NEIGHBOURS
GRAMS_PER_BANK = 4
GBANKS = GROUPS // GRAMS_PER_BANK
H1, H2 = 512, 256
M1, M2 = H1 // 128, H2 // 128
TBANKS = 3
STAGED = 3

COLUMN_GROUPS = [(g - 2, g) for g in range(NEIGHBOURS, 2, -3)] + [(1, 2)]
RTILES = 3
ZROWS = sum(last for _, last in COLUMN_GROUPS)
SHIFTS = len(COLUMN_GROUPS)


def build(nc, ids_gather, ids_onehot, dense_t, tables, identity, select, row_index,
          w_pairs, w_dense, b1, w2, b2, w3, y_out):
    f32, f32r, f16, i32 = mybir.dt.float32, mybir.dt.float32r, mybir.dt.float16, mybir.dt.int32
    ALU, ACT = mybir.AluOpType, mybir.ActivationFunctionType

    with ExitStack() as ctx:
        def sbuf(name, shape, dt):
            return ctx.enter_context(nc.sbuf_tensor(name, shape, dt))

        def sem(name):
            return ctx.enter_context(nc.semaphore(name))

        index = [sbuf(f"index{u}", [128, NGATHER], i32) for u in range(2)]
        rows = [sbuf(f"rows{u}", [128, NGATHER, D], f32) for u in range(2)]
        features = sbuf("features", [128, 2, TILE, SLOT_PITCH], f32)
        blocks = sbuf("blocks", [128, J, NEIGHBOURS, PAIR // J], f32)
        z = sbuf("z", [128, J, RTILES, PAIR // J], f32)
        dense = sbuf("dense", [128, BATCH], f32)
        table_hi = sbuf("table_hi", [128, K1H, KT, D], f32r)
        table_lo = sbuf("table_lo", [128, K1H, KT, D], f32r)
        onehot = sbuf("onehot", [128, 3, KT, PAIR], f32r)
        ids16 = sbuf("ids16", [128, BATCH], f16)
        sel = sbuf("sel", [128, K1H, KROWS], f16)
        row_idx = sbuf("row_idx", [128, KT], f32)
        ident = sbuf("ident", [128, 128], f32)
        w1z = sbuf("w1z", [128, RTILES, H1], f32)
        w1d = sbuf("w1d", [128, H1], f32)
        w2s = sbuf("w2s", [128, M1, H2], f32)
        w3s = sbuf("w3s", [128, M2], f32)
        b1s = sbuf("b1s", [128, M1], f32)
        b2s = sbuf("b2s", [128, M2], f32)
        hidden1 = sbuf("hidden1", [128, M1, PAIR], f32)
        hidden2 = sbuf("hidden2", [128, M2, PAIR], f32)
        looked_up = sbuf("looked_up", [128, STAGED, PAIR], f32)
        y_row = sbuf("y_row", [1, PAIR], f32)
        w1ab = hidden1[:, :, :].rearrange("p m c -> p (m c)").rearrange("p (a n) -> p a n", a=2)
        ids_raw = features[0:K1H, 0, :, :].rearrange("p b f -> p (b f)")[:, 0:BATCH].bitcast(i32)
        table_raw = blocks[:, :, :, :].rearrange("p j g c -> p (j g c)")[:, 0:K1H * KT * D].rearrange(
            "p (k t d) -> p k t d", k=K1H, t=KT)

        t_bank = [ctx.enter_context(nc.psum_tensor(f"t_bank{i}", [128, GRP, TILE], f32)) for i in range(TBANKS)]
        g_bank = [ctx.enter_context(nc.psum_tensor(f"g_bank{i}", [128, 512], f32)) for i in range(2)]
        ids_bank = ctx.enter_context(nc.psum_tensor("ids_bank", [128, 2, PAIR], f32))
        x_bank = [ctx.enter_context(nc.psum_tensor(f"x_bank{i}", [128, 512], f32)) for i in range(2)]

        index_loaded = [sem(f"index_loaded{u}") for u in range(2)]
        gathered = [[sem(f"gathered{u}_{g}") for g in range(NGRP)] for u in range(2)]
        gather_begun = sem("gather_begun")
        onehot_ids_loaded = sem("onehot_ids_loaded")
        sel_loaded = sem("sel_loaded")
        row_idx_loaded = sem("row_idx_loaded")
        ident_loaded = sem("ident_loaded")
        dense_loaded = sem("dense_loaded")
        table_loaded = [sem(f"table_loaded{k}") for k in range(K1H)]
        w1z_loaded = sem("w1z_loaded")
        w1ab_loaded = sem("w1ab_loaded")
        tail_weights_loaded = sem("tail_weights_loaded")
        cleared = sem("cleared")
        ids16_ready = sem("ids16_ready")
        w1d_ready = sem("w1d_ready")
        table_hi_ready = sem("table_hi_ready")
        table_split = sem("table_split")
        ids_spread = sem("ids_spread")
        onehot_made = sem("onehot_made")
        lookup_done = sem("lookup_done")
        lookup_copied = sem("lookup_copied")
        lookup_placed = sem("lookup_placed")
        dense_placed = sem("dense_placed")
        transposed = sem("transposed")
        transpose_copied = sem("transpose_copied")
        gram_done = sem("gram_done")
        gram_copied = [sem("gram_copied_dve"), sem("gram_copied_act")]
        z_shifted = sem("z_shifted")
        h1_summed = sem("h1_summed")
        h1_ready = sem("h1_ready")
        h2_summed = sem("h2_summed")
        h2_ready = sem("h2_ready")
        y_summed = sem("y_summed")
        y_copied = sem("y_copied")
        y_stored = sem("y_stored")

        block = ctx.enter_context(nc.Block())

        def over_pairs(eng, step):
            step(0, True, False)
            with eng.Fori(1, PAIRS - 1) as s:
                step(s, False, False)
            step(PAIRS - 1, False, True)

        def bank_blocks(u, i, j):
            bank = g_bank[i % 2][:, 0:GRAMS_PER_BANK * GRAM_COLS].rearrange(
                "p (t j g) -> p j g t", t=GRAMS_PER_BANK, j=J)
            col = GROUPS * u + GRAMS_PER_BANK * i
            return (bank[SLOT_PITCH * j:SLOT_PITCH * j + NEIGHBOURS, j, :, :],
                    blocks[0:NEIGHBOURS, j, :, col:col + GRAMS_PER_BANK])

        @block.sync
        def _(sp):
            def load_index(tile, u):
                sp.dma_start(index[u][:, :], ids_gather[bass.ds(tile, 1), :, :]
                             .rearrange("a p f -> (a p) f")).then_inc(index_loaded[u], 16)

            def value(x):
                return x if isinstance(x, int) else sp.snap(x)

            load_index(0, 0)
            load_index(1, 1)
            sp.sem_inc(y_stored, 16)
            sp.dma_start(ids_raw, ids_onehot).then_inc(onehot_ids_loaded, 16)
            sp.dma_start(sel[:, :, :], select).then_inc(sel_loaded, 16)
            sp.dma_start(row_idx[0:KROWS, :], row_index).then_inc(row_idx_loaded, 16)
            for k in range(K1H):
                sp.dma_start(table_raw[0:KROWS, k, :, :],
                             tables[ONEHOT_FIELDS[k]].rearrange("(p t) d -> p t d", t=KT)
                             ).then_inc(table_loaded[k], 16)
            sp.dma_start(ident[:, :], identity).then_inc(ident_loaded, 16)
            sp.dma_start(dense[:, :], dense_t).then_inc(dense_loaded, 16)
            sp.dma_start(w1z[0:ZROWS, :, :], w_pairs).then_inc(w1z_loaded, 16)
            sp.dma_start(w1ab, w_dense.rearrange("a p n -> p a n")).then_inc(w1ab_loaded, 16)
            sp.dma_start(w2s[:, :, :], w2.rearrange("(k p) n -> p k n", p=128)).then_inc(tail_weights_loaded, 16)
            sp.dma_start(w3s[:, :], w3).then_inc(tail_weights_loaded, 16)
            sp.dma_start(b1s[:, :], b1).then_inc(tail_weights_loaded, 16)
            sp.dma_start(b2s[:, :], b2).then_inc(tail_weights_loaded, 16)

            def store_y(begin, made):
                sp.wait_ge(y_copied, made)
                sp.dma_start(y_out[bass.ds(begin, PAIR), :].rearrange("(a n) o -> a (n o)", a=1),
                             y_row[:, :]).then_inc(y_stored, 16)

            def step(s, first, last):
                landed = value(16 * GRP * (s + 1))
                next_tile = [value(2 * s + 2 + u) for u in range(2)]
                copied = value(2 * GBANKS * (s + 1))
                y_begin, y_made = value((s - 1) * PAIR), value(s)
                for u in range(2):
                    if not last:
                        for g in range(NGRP):
                            sp.wait_ge(gathered[u][g], landed)
                        load_index(next_tile[u], u)
                sp.wait_ge(gram_copied[0], copied)
                sp.wait_ge(gram_copied[1], copied)
                base = 0
                for lo, hi in COLUMN_GROUPS:
                    n = hi - lo + 1
                    sp.dma_start(z[base:base + hi, :, 0:n, :], blocks[0:hi, :, lo - 1:hi, :]
                                 ).then_inc(z_shifted, 16)
                    base += hi
                if not first:
                    store_y(y_begin, y_made)

            over_pairs(sp, step)
            store_y((PAIRS - 1) * PAIR, PAIRS)
            sp.wait_ge(y_stored, 16 * (PAIRS + 1))

        @block.gpsimd
        def _(pool):
            def step(s, first, last):
                for u in range(2):
                    pool.wait_ge(index_loaded[u], 16 * (s + 1))
                    if not first:
                        pool.wait_ge(transposed, 2 * NGRP * s - NGRP * (1 - u))
                    pool.sem_inc(gather_begun, 1)
                    for n, f in enumerate(GATHER_FIELDS):
                        pool.indirect_dma_start(
                            out=rows[u][:, n, :], out_offset=None, in_=tables[f],
                            in_offset=bass.IndirectOffsetOnAxis(ap=index[u][:, n:n + 1], axis=0)
                        ).then_inc(gathered[u][n // GRP], 16)

            over_pairs(pool, step)

        @block.vector
        def _(dve):
            dve.memset(ids16[:, :], 0.0).then_inc(cleared, 1)
            dve.memset(z[:, :, :, :], 0.0).then_inc(cleared, 1)
            dve.wait_ge(onehot_ids_loaded, 16)
            dve.wait_ge(cleared, 1)
            dve.tensor_copy(ids16[0:K1H, :], ids_raw).then_inc(ids16_ready, 1)
            dve.wait_ge(ids16_ready, 1)
            dve.memset(features[:, :, :, FEATURES:SLOT_PITCH], 0.0).then_inc(cleared, 1)
            for k in range(K1H):
                dve.wait_ge(table_hi_ready, k + 1)
                dve.tensor_tensor(table_lo[0:KROWS, k, :, :], table_raw[0:KROWS, k, :, :],
                                  table_hi[0:KROWS, k, :, :].bitcast(f32), ALU.subtract).then_inc(table_split, 1)
            dve.wait_ge(w1ab_loaded, 16)
            dve.tensor_tensor(w1d[:, :], w1ab[:, 0, :], w1ab[:, 1, :], ALU.add).then_inc(w1d_ready, 1)
            dve.wait_ge(row_idx_loaded, 16)

            def make_onehot(s, k, first):
                dve.wait_ge(ids_spread, (K1H // 2) * s + k // 2 + 1)
                if not (first and k < 3):
                    dve.wait_ge(lookup_done, K1H * s + k - 2)
                dve.tensor_tensor(
                    onehot[0:KROWS, k % 3, :, :],
                    ids_bank[0:KROWS, k % 2, :].unsqueeze(1).broadcast_to([KROWS, KT, PAIR]),
                    row_idx[0:KROWS, :].unsqueeze(2).broadcast_to([KROWS, KT, PAIR]),
                    ALU.is_equal).then_inc(onehot_made, 1)

            def copy_blocks(s, u, first):
                if u == 0 and not first:
                    dve.wait_ge(z_shifted, 16 * SHIFTS * s)
                for i in range(GBANKS):
                    dve.wait_ge(gram_done, 2 * GBANKS * s + GBANKS * u + i + 1)
                    for j in range(J // 2):
                        source, place = bank_blocks(u, i, j)
                        last_copy = dve.tensor_copy(place, source)
                    last_copy.then_inc(gram_copied[0], 1)

            def step(s, first, last):
                copy_blocks(s, 0, first)
                if not last:
                    for k in range(5):
                        make_onehot(s + 1, k, False)
                copy_blocks(s, 1, first)
                if not last:
                    for k in range(5, K1H):
                        make_onehot(s + 1, k, False)

            for k in range(K1H):
                make_onehot(0, k, True)
            over_pairs(dve, step)

        @block.scalar
        def _(act):
            for k in range(K1H):
                act.wait_ge(table_loaded[k], 16)
                act.activation(table_hi[0:KROWS, k, :, :], table_raw[0:KROWS, k, :, :],
                               ACT.Copy).then_inc(table_hi_ready, 1)
            act.wait_ge(dense_loaded, 16)
            act.wait_ge(tail_weights_loaded, 64)

            def slot(i):
                return features[:, :, :, i].rearrange("d u (t j) -> d j u t", j=J)

            def in_order(cols):
                return cols.rearrange("d (j u t) -> d j u t", j=J, u=2)

            def copy_transposes(s, u):
                for g in range(NGRP):
                    act.wait_ge(transposed, NGRP * (2 * s + u) + g + 1)
                    act.activation(features[:, u, :, 1 + GRP * g:1 + GRP * (g + 1)],
                                   t_bank[g % TBANKS][:, :, :].rearrange("d f p -> d p f"),
                                   ACT.Copy).then_inc(transpose_copied, 1)

            def copy_blocks(s, u, first):
                if u == 0 and not first:
                    act.wait_ge(z_shifted, 16 * SHIFTS * s)
                for i in range(GBANKS):
                    act.wait_ge(gram_done, 2 * GBANKS * s + GBANKS * u + i + 1)
                    for j in range(J // 2, J):
                        source, place = bank_blocks(u, i, j)
                        last_copy = act.activation(place, source, ACT.Copy)
                    last_copy.then_inc(gram_copied[1], 1)

            def relu1(s, quarters):
                for m in quarters:
                    act.wait_ge(h1_summed, M1 * s + m + 1)
                    act.activation(hidden1[:, m, :], x_bank[m % 2][:, 0:PAIR], ACT.Relu,
                                   bias=b1s[:, m:m + 1]).then_inc(h1_ready, 1)

            def relu2(s):
                for m in range(M2):
                    act.wait_ge(h2_summed, M2 * s + m + 1)
                    act.activation(hidden2[:, m, :], x_bank[m][:, 0:PAIR], ACT.Relu,
                                   bias=b2s[:, m:m + 1]).then_inc(h2_ready, 1)

            def copy_y(s):
                act.wait_ge(y_summed, s + 1)
                act.wait_ge(y_stored, 16 * (s + 1))
                act.activation(y_row[:, :], x_bank[1][0:1, 0:PAIR], ACT.Copy).then_inc(y_copied, 1)

            def place_dense(s):
                act.activation(slot(0), in_order(dense[:, bass.ds(s * PAIR, PAIR)]),
                               ACT.Copy).then_inc(dense_placed, 1)

            def copy_lookup(s, k, out):
                act.wait_ge(lookup_done, K1H * s + k + 1)
                act.activation(out, in_order(x_bank[LOOKUP_BANK[k]][:, 0:PAIR]),
                               ACT.Copy).then_inc(lookup_copied, 1)

            def stage_lookup(s, k):
                copy_lookup(s, k, in_order(looked_up[:, k, :]))

            def step(s, first, last):
                copy_transposes(s, 0)
                if not first:
                    relu1(s - 1, range(1))
                copy_blocks(s, 0, first)
                if not first:
                    relu1(s - 1, range(1, M1))
                if not last:
                    stage_lookup(s + 1, 0)
                copy_transposes(s, 1)
                if last:
                    copy_blocks(s, 1, first)
                else:
                    stage_lookup(s + 1, 1)
                if not first:
                    relu2(s - 1)
                if not last:
                    stage_lookup(s + 1, 2)
                if not first:
                    copy_y(s - 1)
                if not last:
                    copy_blocks(s, 1, first)
                    act.wait_ge(gram_done, 2 * GBANKS * (s + 1))
                    act.wait_ge(lookup_copied, K1H * (s + 1) + STAGED)
                    for k in range(STAGED):
                        act.activation(slot(1 + NGATHER + k), in_order(looked_up[:, k, :]),
                                       ACT.Copy).then_inc(lookup_placed, 1)
                    place_dense(s + 1)
                    for k in range(STAGED, K1H):
                        copy_lookup(s + 1, k, slot(1 + NGATHER + k))

            act.wait_ge(ids16_ready, 1)
            place_dense(0)
            for k in range(K1H):
                copy_lookup(0, k, slot(1 + NGATHER + k))
            over_pairs(act, step)
            relu1(PAIRS - 1, range(M1))
            relu2(PAIRS - 1)
            copy_y(PAIRS - 1)

        @block.tensor
        def _(pe):
            def spread_ids(s, q, first):
                if not (first and q == 0):
                    pe.wait_ge(onehot_made, K1H * s + 2 * q)
                for i in range(2):
                    last_mm = pe.matmul(ids_bank[0:KROWS, i, :], sel[:, 2 * q + i, :],
                                        ids16[:, bass.ds(s * PAIR, PAIR)], start=True, stop=True)
                last_mm.then_inc(ids_spread, 1)

            def look_up(s, k, first):
                pe.wait_ge(onehot_made, K1H * s + k + 1)
                if first:
                    pe.wait_ge(table_split, k + 1)
                for kt in range(KT):
                    for part, table in enumerate((table_hi, table_lo)):
                        last_mm = pe.matmul(x_bank[LOOKUP_BANK[k]][:, 0:PAIR], table[0:KROWS, k, kt, :],
                                            onehot[0:KROWS, k % 3, kt, :],
                                            start=kt + part == 0, stop=kt + part == KT)
                last_mm.then_inc(lookup_done, 1)

            def transpose_rows(s, u, first):
                for g in range(NGRP):
                    pe.wait_ge(gathered[u][g], 16 * GRP * (s + 1))
                    if g >= TBANKS:
                        pe.wait_ge(transpose_copied, 2 * NGRP * s + NGRP * u + g - TBANKS + 1)
                    for i in range(GRP):
                        last_mm = pe.transpose(t_bank[g % TBANKS][:, i, :], rows[u][:, GRP * g + i, :], ident[:, :])
                    last_mm.then_inc(transposed, 1)

            def multiply_features(s, u, first):
                pe.wait_ge(transpose_copied, NGRP * (2 * s + u + 1))
                pe.wait_ge(lookup_copied, K1H * (s + 1))
                if not first:
                    pe.wait_ge(lookup_placed, STAGED * s)
                pe.wait_ge(dense_placed, s + 1)
                for i in range(GBANKS):
                    n = GBANKS * u + i
                    if not (first and n < 2):
                        pe.wait_ge(gram_copied[0], 2 * GBANKS * s + n - 1)
                        pe.wait_ge(gram_copied[1], 2 * GBANKS * s + n - 1)
                    for t in range(GRAMS_PER_BANK):
                        p = J * (GRAMS_PER_BANK * i + t)
                        last_mm = pe.matmul(
                            g_bank[i % 2][:, GRAM_COLS * t:GRAM_COLS * (t + 1)],
                            features[:, u, p:p + J, :].rearrange("d j f -> d (j f)"),
                            features[:, u, p:p + J, 1:FEATURES], start=True, stop=True)
                    last_mm.then_inc(gram_done, 1)

            def layer1(s, m):
                if m == 0:
                    pe.wait_ge(z_shifted, 16 * SHIFTS * (s + 1))
                if m >= 2:
                    pe.wait_ge(h1_ready, M1 * s + m - 1)
                cols = slice(128 * m, 128 * (m + 1))
                pe.matmul(x_bank[m % 2][:, 0:PAIR], w1d[:, cols], dense[:, bass.ds(s * PAIR, PAIR)],
                          start=True, stop=False)
                for r in range(RTILES):
                    last_mm = pe.matmul(x_bank[m % 2][:, 0:PAIR], w1z[0:ZROWS, r, cols],
                                        z[0:ZROWS, :, r, :], start=False, stop=r == RTILES - 1)
                last_mm.then_inc(h1_summed, 1)

            def layer2(s, m):
                pe.wait_ge(h1_ready, M1 * (s + 1))
                for k in range(M1):
                    last_mm = pe.matmul(x_bank[m][:, 0:PAIR], w2s[:, k, 128 * m:128 * (m + 1)],
                                        hidden1[:, k, :], start=k == 0, stop=k == M1 - 1)
                last_mm.then_inc(h2_summed, 1)

            def layer3(s):
                pe.wait_ge(h2_ready, M2 * (s + 1))
                for k in range(M2):
                    last_mm = pe.matmul(x_bank[1][0:1, 0:PAIR], w3s[:, k:k + 1], hidden2[:, k, :],
                                        start=k == 0, stop=k == M2 - 1)
                last_mm.then_inc(y_summed, 1)

            def step(s, first, last):
                transpose_rows(s, 0, first)
                if not first:
                    pe.wait_ge(lookup_copied, K1H * (s + 1))
                    layer1(s - 1, 0)
                multiply_features(s, 0, first)
                if not last:
                    spread_ids(s + 1, 0, False)
                if not first:
                    for m in range(1, M1):
                        layer1(s - 1, m)
                if not last:
                    spread_ids(s + 1, 1, False)
                    if not first:
                        pe.wait_ge(h1_ready, M1 * s - 1)
                    look_up(s + 1, 0, False)
                transpose_rows(s, 1, first)
                if last:
                    multiply_features(s, 1, first)
                else:
                    if not first:
                        pe.wait_ge(h1_ready, M1 * s)
                    look_up(s + 1, 1, False)
                    spread_ids(s + 1, 2, False)
                    pe.wait_ge(lookup_copied, K1H * (s + 1) + 1)
                if not first:
                    layer2(s - 1, 0)
                    if not last:
                        pe.wait_ge(lookup_copied, K1H * (s + 1) + 2)
                    layer2(s - 1, 1)
                if not last:
                    if not first:
                        pe.wait_ge(h2_ready, M2 * s - 1)
                    look_up(s + 1, 2, False)
                if not first:
                    layer3(s - 1)
                if not last:
                    multiply_features(s, 1, first)
                    pe.wait_ge(lookup_copied, K1H * (s + 1) + 3)
                    look_up(s + 1, 3, False)
                    if first:
                        pe.wait_ge(lookup_copied, K1H * (s + 1) + 2)
                    else:
                        pe.wait_ge(y_copied, s)
                    look_up(s + 1, 4, False)
                    pe.wait_ge(lookup_copied, K1H * (s + 1) + 4)
                    look_up(s + 1, 5, False)

            pe.wait_ge(sel_loaded, 16)
            pe.wait_ge(ids16_ready, 1)
            pe.wait_ge(cleared, 3)
            for k in range(K1H):
                if k % 2 == 0:
                    spread_ids(0, k // 2, True)
                if k >= 2:
                    pe.wait_ge(lookup_copied, k)
                look_up(0, k, True)
            pe.wait_ge(ident_loaded, 16)
            pe.wait_ge(w1z_loaded, 16)
            pe.wait_ge(w1d_ready, 1)
            pe.wait_ge(tail_weights_loaded, 64)
            over_pairs(pe, step)
            pe.wait_ge(y_copied, PAIRS - 1)
            for m in range(M1):
                layer1(PAIRS - 1, m)
            for m in range(M2):
                layer2(PAIRS - 1, m)
            layer3(PAIRS - 1)


def pair_weight_rows():
    feature = (0,) + tuple(f + 1 for f in GATHER_FIELDS) + tuple(f + 1 for f in ONEHOT_FIELDS)
    at = []
    for lo, hi in COLUMN_GROUPS:
        for left in range(hi):
            line = []
            for right in range(lo, lo + RTILES):
                if left < right <= hi:
                    a, b = sorted((feature[left], feature[right]))
                    line.append(D + a * (2 * FEATURES - a - 1) // 2 + b - a - 1)
                else:
                    line.append(-1)
            at.append(line)
    return at


def kernel(**inputs):
    import numpy as np
    import concourse.bacc as bacc
    from concourse.bass_utils import run_bass_kernel_spmd

    ids = np.asarray(inputs["ids"])
    w1 = np.asarray(inputs["W_top1"])
    at = np.array(pair_weight_rows())
    w_pairs = np.zeros((ZROWS, RTILES, H1), w1.dtype)
    w_pairs[at >= 0] = w1[at[at >= 0]]
    select = np.zeros((128, K1H, KROWS), np.float16)
    for k in range(K1H):
        select[k, k, :] = 1.0
    by_tile = ids.reshape(PAIRS, J, 2, GROUPS, FIELDS).transpose(0, 2, 3, 1, 4)
    arrays = {
        "ids_gather": by_tile[..., list(GATHER_FIELDS)].reshape(2 * PAIRS, TILE, NGATHER),
        "ids_onehot": ids[:, list(ONEHOT_FIELDS)].T,
        "dense_t": np.asarray(inputs["r_dense_output"]).T,
        "identity": np.eye(128, dtype=np.float32),
        "select": select,
        "row_index": np.arange(ROWS_1000, dtype=np.float32).reshape(KROWS, KT),
        "w_pairs": w_pairs,
        "w_dense": np.stack([w1[:D], w1[-D:]]),
        "b1": np.asarray(inputs["b_top1"]).reshape(M1, 128).T,
        "w2": np.asarray(inputs["W_top2"]),
        "b2": np.asarray(inputs["b_top2"]).reshape(M2, 128).T,
        "w3": np.asarray(inputs["W_top3"]).reshape(M2, 128).T,
    }
    arrays |= {f"tbl_{f}": np.asarray(inputs[f"tbl_{f}"]) for f in range(FIELDS)}
    arrays = {name: np.ascontiguousarray(a) for name, a in arrays.items()}

    nc = bacc.Bacc("TRN2", target_bir_lowering=False, num_devices=1)
    ap = {name: nc.dram_tensor(name, a.shape, mybir.dt.from_np(a.dtype), kind="ExternalInput").ap()
          for name, a in arrays.items()}
    y = nc.dram_tensor("y", (BATCH, 1), mybir.dt.float32, kind="ExternalOutput").ap()
    build(nc, ap["ids_gather"], ap["ids_onehot"], ap["dense_t"], [ap[f"tbl_{f}"] for f in range(FIELDS)],
          ap["identity"], ap["select"], ap["row_index"], ap["w_pairs"], ap["w_dense"], ap["b1"], ap["w2"],
          ap["b2"], ap["w3"], y)
    return run_bass_kernel_spmd(nc, [arrays], core_ids=[0]).results[0]["y"]
```

```python
from contextlib import ExitStack

import concourse.bass as bass
from concourse import mybir

BATCH, FIELDS, D = 2048, 26, 128
ROWS_1000, ROWS_1250 = 1000, 1250
LOOKUP_BANK = (0, 1, 0, 0, 1, 0)
ONEHOT_FIELDS = (2, 16, 17, 18, 24, 25)
ROW_FIELD = 1
GATHER_FIELDS = tuple(f for f in range(FIELDS) if f not in ONEHOT_FIELDS + (ROW_FIELD,)) + (ROW_FIELD,)
K1H, NGATHER = len(ONEHOT_FIELDS), len(GATHER_FIELDS)
FEATURES = FIELDS + 1
SLOT_PITCH = 32
TILE, PAIR = 128, 256
PAIRS = BATCH // PAIR
J = 4
GROUPS = TILE // J
GRP = 4
NGRP = NGATHER // GRP
KT, KROWS = 8, ROWS_1000 // 8
RT = ROWS_1250 // KROWS
ROW_BANK = 2
NEIGHBOURS = FEATURES - 1
GRAM_COLS = J * NEIGHBOURS
GRAM_ROWS = (J - 1) * SLOT_PITCH + NEIGHBOURS
GRAMS_PER_BANK = 4
GBANKS = GROUPS // GRAMS_PER_BANK
H1, H2 = 512, 256
M1, M2 = H1 // 128, H2 // 128
TBANKS = 3
STAGED = 3

COLUMN_GROUPS = [(g - 2, g) for g in range(NEIGHBOURS, 2, -3)] + [(1, 2)]
RTILES = 3
ZROWS = sum(last for _, last in COLUMN_GROUPS)
SHIFTS = len(COLUMN_GROUPS)
POOL_SHIFTS = 2


def build(nc, ids_gather, ids_onehot, dense_t, tables, identity, row_index,
          w_pairs, w_dense, b1, w2, b2, w3, y_out):
    f32, f32r, i32 = mybir.dt.float32, mybir.dt.float32r, mybir.dt.int32
    ALU, ACT = mybir.AluOpType, mybir.ActivationFunctionType

    with ExitStack() as ctx:
        def sbuf(name, shape, dt):
            return ctx.enter_context(nc.sbuf_tensor(name, shape, dt))

        def sem(name):
            return ctx.enter_context(nc.semaphore(name))

        index = [sbuf(f"index{u}", [128, NGATHER], i32) for u in range(2)]
        rows = [sbuf(f"rows{u}", [128, NGATHER, D], f32) for u in range(2)]
        features = sbuf("features", [128, 2, TILE, SLOT_PITCH], f32)
        blocks = sbuf("blocks", [128, 2, J, NEIGHBOURS, GROUPS], f32)
        z = sbuf("z", [128, 2, J, RTILES, GROUPS], f32)
        dense = sbuf("dense", [128, BATCH], f32)
        table_hi = sbuf("table_hi", [128, K1H, KT, D], f32r)
        table_lo = sbuf("table_lo", [128, K1H, KT, D], f32r)
        onehot = sbuf("onehot", [128, 3, KT, PAIR], f32r)
        ids = sbuf("ids", [128, K1H * PAIR + TILE], i32)
        row_idx = sbuf("row_idx", [128, KT + RT], i32)
        row_table = sbuf("row_table", [128, RT, 2, D], f32r)
        row_onehot = sbuf("row_onehot", [128, RT, TILE], f32r)
        ident = sbuf("ident", [128, 128], f32)
        w1z = sbuf("w1z", [128, RTILES, H1], f32)
        w1d = sbuf("w1d", [128, H1], f32)
        w2s = sbuf("w2s", [128, M1, H2], f32)
        w3s = sbuf("w3s", [128, M2], f32)
        b1s = sbuf("b1s", [128, M1], f32)
        b2s = sbuf("b2s", [128, M2], f32)
        hidden1 = sbuf("hidden1", [128, M1, PAIR], f32)
        hidden2 = sbuf("hidden2", [128, M2, PAIR], f32)
        looked_up = sbuf("looked_up", [128, STAGED, PAIR], f32)
        y_row = sbuf("y_row", [1, PAIR], f32)
        w1ab = hidden1[:, :, :].rearrange("p m c -> p (m c)").rearrange("p (a n) -> p a n", a=2)
        table_raw = blocks[:, :, :, :, :].rearrange("p u j g t -> p (u j g t)")[:, 0:K1H * KT * D].rearrange(
            "p (k t d) -> p k t d", k=K1H, t=KT)
        row_raw = [(0, looked_up[:, :, :].rearrange("p m (t d) -> p (m t) d", d=D)),
                   (2 * STAGED, hidden2[:, :, :].rearrange("p m (t d) -> p (m t) d", d=D))]

        t_bank = [ctx.enter_context(nc.psum_tensor(f"t_bank{i}", [128, GRP, TILE], f32)) for i in range(TBANKS)]
        g_bank = [ctx.enter_context(nc.psum_tensor(f"g_bank{i}", [128, 512], f32)) for i in range(2)]
        x_bank = [ctx.enter_context(nc.psum_tensor(f"x_bank{i}", [128, 512], f32)) for i in range(2)]

        h1_bank = [x_bank, g_bank]
        h2_bank = [t_bank[m][:, 0, :] for m in range(M2)]
        y_bank = [t_bank[2][0:1, 0, :], x_bank[0][0:1, 0:TILE]]

        row_parts = t_bank[ROW_BANK][:, 0:2, :]

        index_loaded = [sem(f"index_loaded{u}") for u in range(2)]
        gathered = [[sem(f"gathered{u}_{g}") for g in range(NGRP)] for u in range(2)]
        gather_begun = sem("gather_begun")
        ids_loaded = sem("ids_loaded")
        row_idx_loaded = sem("row_idx_loaded")
        ident_loaded = sem("ident_loaded")
        dense_loaded = sem("dense_loaded")
        table_loaded = [sem(f"table_loaded{k}") for k in range(K1H)]
        w1z_loaded = sem("w1z_loaded")
        w1ab_loaded = sem("w1ab_loaded")
        tail_weights_loaded = sem("tail_weights_loaded")
        cleared = sem("cleared")
        w1d_ready = sem("w1d_ready")
        table_hi_ready = sem("table_hi_ready")
        table_split = sem("table_split")
        row_table_loaded = [sem(f"row_table_loaded{i}") for i in range(2)]
        row_hi_ready = sem("row_hi_ready")
        row_table_split = sem("row_table_split")
        row_onehot_made = sem("row_onehot_made")
        row_looked_up = sem("row_looked_up")
        row_placed = sem("row_placed")
        onehot_made = sem("onehot_made")
        lookup_done = sem("lookup_done")
        lookup_copied = sem("lookup_copied")
        lookup_placed = sem("lookup_placed")
        dense_placed = sem("dense_placed")
        transposed = sem("transposed")
        transpose_copied = sem("transpose_copied")
        gram_done = sem("gram_done")
        gram_copied = [sem("gram_copied_dve"), sem("gram_copied_act")]
        z_shifted = sem("z_shifted")
        z_half_shifted = [sem(f"z_half_shifted{u}") for u in range(2)]
        z_half_shifted_by_pool = sem("z_half_shifted_by_pool")
        h1_summed = sem("h1_summed")
        h1_ready = sem("h1_ready")
        h2_summed = sem("h2_summed")
        h2_ready = sem("h2_ready")
        y_summed = sem("y_summed")
        y_copied = sem("y_copied")
        y_stored = sem("y_stored")

        block = ctx.enter_context(nc.Block())

        def over_pairs(eng, step):
            step(0, True, False)
            with eng.Fori(1, PAIRS - 1) as s:
                step(s, False, False)
            step(PAIRS - 1, False, True)

        def bank_blocks(u, i, j):
            bank = g_bank[i % 2][:, 0:GRAMS_PER_BANK * GRAM_COLS].rearrange(
                "p (t j g) -> p j g t", t=GRAMS_PER_BANK, j=J)
            col = GRAMS_PER_BANK * i
            return (bank[SLOT_PITCH * j:SLOT_PITCH * j + NEIGHBOURS, j, :, :],
                    blocks[0:NEIGHBOURS, u, j, :, col:col + GRAMS_PER_BANK])

        first_row = [sum(last for _, last in COLUMN_GROUPS[:c]) for c in range(SHIFTS)]

        def packed_rows(c, begin, end):
            lo, hi = COLUMN_GROUPS[c]
            return (z[first_row[c]:first_row[c] + hi, begin:end, :, 0:hi - lo + 1, :],
                    blocks[0:hi, begin:end, :, lo - 1:hi, :])

        @block.sync
        def _(sp):
            def load_index(tile, u):
                sp.dma_start(index[u][:, :], ids_gather[bass.ds(tile, 1), :, :]
                             .rearrange("a p f -> (a p) f")).then_inc(index_loaded[u], 16)

            def load_ids(pair):
                sp.dma_start(ids[:, :], ids_onehot[bass.ds(pair, 1), :].broadcast_to([128, K1H * PAIR + TILE])
                             ).then_inc(ids_loaded, 16)

            def value(x):
                return x if isinstance(x, int) else sp.snap(x)

            load_index(0, 0)
            load_index(1, 1)
            sp.sem_inc(y_stored, 16)
            load_ids(0)
            sp.dma_start(row_idx[0:KROWS, :], row_index).then_inc(row_idx_loaded, 16)
            for k in range(K1H):
                sp.dma_start(table_raw[0:KROWS, k, :, :],
                             tables[ONEHOT_FIELDS[k]].rearrange("(p t) d -> p t d", t=KT)
                             ).then_inc(table_loaded[k], 16)
            table = tables[ROW_FIELD].rearrange("(p t) d -> p t d", t=RT)
            for i, (begin, room) in enumerate(row_raw):
                end = min(begin + room.shape[1], RT)
                sp.dma_start(room[0:KROWS, 0:end - begin, :], table[:, begin:end, :]
                             ).then_inc(row_table_loaded[i], 16)
            sp.dma_start(ident[:, :], identity).then_inc(ident_loaded, 16)
            sp.dma_start(dense[:, :], dense_t).then_inc(dense_loaded, 16)
            sp.dma_start(w1z[0:ZROWS, :, :], w_pairs).then_inc(w1z_loaded, 16)
            sp.dma_start(w1ab, w_dense.rearrange("a p n -> p a n")).then_inc(w1ab_loaded, 16)
            sp.dma_start(w2s[:, :, :], w2.rearrange("(k p) n -> p k n", p=128)).then_inc(tail_weights_loaded, 16)
            sp.dma_start(w3s[:, :], w3).then_inc(tail_weights_loaded, 16)
            sp.dma_start(b1s[:, :], b1).then_inc(tail_weights_loaded, 16)
            sp.dma_start(b2s[:, :], b2).then_inc(tail_weights_loaded, 16)
            sp.wait_ge(onehot_made, K1H)
            load_ids(1)

            def store_y(begin, made):
                sp.wait_ge(y_copied, made)
                sp.dma_start(y_out[bass.ds(begin, PAIR), :].rearrange("(a n) o -> a (n o)", a=1),
                             y_row[:, :]).then_inc(y_stored, 16)

            def step(s, load_more):
                rows_used = [value(2 * NGRP * s + NGRP * (1 + u)) for u in range(2)]
                next_tile = [value(2 * s + 2 + u) for u in range(2)]
                copied = value(2 * GBANKS * (s + 1))
                y_begin, y_made = value((s - 1) * PAIR), value(s)
                onehots, row_onehots, next_ids = value(K1H * (s + 2)), value(s + 1), value(s + 2)
                for u in range(2):
                    sp.wait_ge(transposed, rows_used[u])
                    load_index(next_tile[u], u)
                sp.wait_ge(gram_copied[0], copied)
                sp.wait_ge(gram_copied[1], copied)
                for c in range(SHIFTS):
                    place, source = packed_rows(c, 0, 2)
                    sp.dma_start(place, source).then_inc(z_shifted, 16)
                if load_more:
                    sp.wait_ge(onehot_made, onehots)
                    sp.wait_ge(row_onehot_made, row_onehots)
                    load_ids(next_ids)
                if not (isinstance(s, int) and s == 0):
                    store_y(y_begin, y_made)

            step(0, True)
            with sp.Fori(1, PAIRS - 2) as s:
                step(s, True)
            step(PAIRS - 2, False)
            last = PAIRS - 1
            sp.wait_ge(gram_copied[0], 2 * GBANKS * last + GBANKS)
            sp.wait_ge(gram_copied[1], 2 * GBANKS * last + GBANKS)
            sp.wait_ge(h1_summed, M1 * last)
            for c in range(SHIFTS):
                place, source = packed_rows(c, 0, 1)
                sp.dma_start(place, source).then_inc(z_half_shifted[0], 16)
            store_y((last - 1) * PAIR, last)
            sp.wait_ge(gram_copied[0], 2 * GBANKS * PAIRS)
            sp.wait_ge(gram_copied[1], 2 * GBANKS * PAIRS)
            for c in range(SHIFTS - POOL_SHIFTS):
                place, source = packed_rows(c, 1, 2)
                sp.dma_start(place, source).then_inc(z_half_shifted[1], 16)
            store_y(last * PAIR, PAIRS + 1)
            sp.wait_ge(y_stored, 16 * (PAIRS + 1))

        @block.gpsimd
        def _(pool):
            def step(s, first, last):
                for u in range(2):
                    pool.wait_ge(index_loaded[u], 16 * (s + 1))
                    if not first:
                        pool.wait_ge(transposed, 2 * NGRP * s - NGRP * (1 - u))
                    pool.sem_inc(gather_begun, 1)
                    for n, f in enumerate(GATHER_FIELDS if first or u == 1 else GATHER_FIELDS[:-1]):
                        pool.indirect_dma_start(
                            out=rows[u][:, n, :], out_offset=None, in_=tables[f],
                            in_offset=bass.IndirectOffsetOnAxis(ap=index[u][:, n:n + 1], axis=0)
                        ).then_inc(gathered[u][n // GRP], 16)

            over_pairs(pool, step)
            pool.wait_ge(gram_copied[0], 2 * GBANKS * PAIRS)
            pool.wait_ge(gram_copied[1], 2 * GBANKS * PAIRS)
            for c in range(SHIFTS - POOL_SHIFTS, SHIFTS):
                place, source = packed_rows(c, 1, 2)
                pool.dma_start(place, source).then_inc(z_half_shifted_by_pool, 16)

        @block.vector
        def _(dve):
            dve.memset(features[:, :, :, FEATURES:SLOT_PITCH], 0.0).then_inc(cleared, 1)
            dve.memset(z[:, :, :, :, :], 0.0).then_inc(cleared, 1)
            dve.wait_ge(row_idx_loaded, 16)

            def split_table(k):
                dve.wait_ge(table_hi_ready, k + 1)
                dve.tensor_tensor(table_lo[0:KROWS, k, :, :], table_raw[0:KROWS, k, :, :],
                                  table_hi[0:KROWS, k, :, :].bitcast(f32), ALU.subtract).then_inc(table_split, 1)

            def make_onehot(s, k, first):
                dve.wait_ge(ids_loaded, 16 * (s + 1))
                if not (first and k < 3):
                    dve.wait_ge(lookup_done, K1H * s + k - 2)
                dve.tensor_tensor(
                    onehot[0:KROWS, k % 3, :, :],
                    ids[0:KROWS, PAIR * k:PAIR * (k + 1)].unsqueeze(1).broadcast_to([KROWS, KT, PAIR]),
                    row_idx[0:KROWS, 0:KT].unsqueeze(2).broadcast_to([KROWS, KT, PAIR]),
                    ALU.is_equal).then_inc(onehot_made, 1)

            def make_row_onehot(s):
                dve.wait_ge(ids_loaded, 16 * (s + 1))
                dve.tensor_tensor(
                    row_onehot[0:KROWS, :, :],
                    ids[0:KROWS, K1H * PAIR:K1H * PAIR + TILE].unsqueeze(1).broadcast_to([KROWS, RT, TILE]),
                    row_idx[0:KROWS, KT:KT + RT].unsqueeze(2).broadcast_to([KROWS, RT, TILE]),
                    ALU.is_equal).then_inc(row_onehot_made, 1)

            def place_rows(s):
                dve.wait_ge(row_looked_up, s)
                dve.wait_ge(transposed, 2 * NGRP * s - NGRP)
                dve.tensor_reduce(rows[0][:, NGATHER - 1, :], row_parts.rearrange("p i d -> p d i"),
                                  op=ALU.add, axis=mybir.AxisListType.X).then_inc(row_placed, 1)

            def copy_blocks(s, u, first):
                if u == 0 and not first:
                    dve.wait_ge(z_shifted, 16 * SHIFTS * s)
                for i in range(GBANKS):
                    dve.wait_ge(gram_done, 2 * GBANKS * s + GBANKS * u + i + 1)
                    for j in range(J // 2):
                        source, place = bank_blocks(u, i, j)
                        last_copy = dve.tensor_copy(place, source)
                    last_copy.then_inc(gram_copied[0], 1)

            def step(s, first, last):
                if first:
                    make_onehot(1, 0, False)
                    make_onehot(1, 1, False)
                copy_blocks(s, 0, first)
                if not last:
                    for k in range(2 if first else 0, 2):
                        make_onehot(s + 1, k, False)
                    make_row_onehot(s + 1)
                    for k in range(2, 5):
                        make_onehot(s + 1, k, False)
                    place_rows(s + 1)
                copy_blocks(s, 1, first)
                if not last:
                    for k in range(5, K1H):
                        make_onehot(s + 1, k, False)

            for k in range(K1H):
                make_onehot(0, k, True)
                split_table(k)
            for i, (begin, room) in enumerate(row_raw):
                end = min(begin + room.shape[1], RT)
                dve.wait_ge(row_hi_ready, i + 1)
                dve.tensor_tensor(row_table[0:KROWS, begin:end, 1, :], room[0:KROWS, 0:end - begin, :],
                                  row_table[0:KROWS, begin:end, 0, :].bitcast(f32),
                                  ALU.subtract).then_inc(row_table_split, 1)
            dve.wait_ge(w1ab_loaded, 16)
            dve.tensor_tensor(w1d[:, :], w1ab[:, 0, :], w1ab[:, 1, :], ALU.add).then_inc(w1d_ready, 1)
            over_pairs(dve, step)

        @block.scalar
        def _(act):
            for k in range(K1H):
                act.wait_ge(table_loaded[k], 16)
                act.activation(table_hi[0:KROWS, k, :, :], table_raw[0:KROWS, k, :, :],
                               ACT.Copy).then_inc(table_hi_ready, 1)

            def round_row_table():
                for i, (begin, room) in enumerate(row_raw):
                    end = min(begin + room.shape[1], RT)
                    act.wait_ge(row_table_loaded[i], 16)
                    act.activation(row_table[0:KROWS, begin:end, 0, :], room[0:KROWS, 0:end - begin, :],
                                   ACT.Copy).then_inc(row_hi_ready, 1)

            def slot(i):
                return features[:, :, :, i].rearrange("d u (t j) -> d j u t", j=J)

            def in_order(cols):
                return cols.rearrange("d (j u t) -> d j u t", j=J, u=2)

            def copy_transposes(s, u, groups=range(NGRP)):
                for g in groups:
                    act.wait_ge(transposed, NGRP * (2 * s + u) + g + 1)
                    act.activation(features[:, u, :, 1 + GRP * g:1 + GRP * (g + 1)],
                                   t_bank[g % TBANKS][:, :, :].rearrange("d f p -> d p f"),
                                   ACT.Copy).then_inc(transpose_copied, 1)

            def copy_blocks(s, u, first):
                if u == 0 and not first:
                    act.wait_ge(z_shifted, 16 * SHIFTS * s)
                for i in range(GBANKS):
                    act.wait_ge(gram_done, 2 * GBANKS * s + GBANKS * u + i + 1)
                    for j in range(J // 2, J):
                        source, place = bank_blocks(u, i, j)
                        last_copy = act.activation(place, source, ACT.Copy)
                    last_copy.then_inc(gram_copied[1], 1)

            def relu1(s, quarters, n=PAIR, bank=x_bank):
                for m in quarters:
                    act.wait_ge(h1_summed, M1 * s + m + 1)
                    act.activation(hidden1[:, m, 0:n], bank[m % 2][:, 0:n], ACT.Relu,
                                   bias=b1s[:, m:m + 1]).then_inc(h1_ready, 1)

            def relu2(s, halves=range(M2), n=PAIR, bank=x_bank):
                for m in halves:
                    act.wait_ge(h2_summed, M2 * s + m + 1)
                    act.activation(hidden2[:, m, 0:n], bank[m][:, 0:n], ACT.Relu,
                                   bias=b2s[:, m:m + 1]).then_inc(h2_ready, 1)

            def y_tiles(begin, end):
                return y_row[:, :].rearrange("a (j u t) -> a u j t", j=J, u=2)[:, begin:end, :, :]

            def unit_cols(cols):
                return cols.rearrange("a (u j t) -> a u j t", j=J, t=GROUPS)

            def copy_y(s):
                act.wait_ge(y_summed, s + 1)
                act.wait_ge(y_stored, 16 * (s + 1))
                act.activation(y_tiles(0, 2), unit_cols(x_bank[1][0:1, 0:PAIR]), ACT.Copy).then_inc(y_copied, 1)

            def place_dense(s):
                act.activation(slot(0), in_order(dense[:, bass.ds(s * PAIR, PAIR)]),
                               ACT.Copy).then_inc(dense_placed, 1)

            def copy_lookup(s, k, out):
                act.wait_ge(lookup_done, K1H * s + k + 1)
                act.activation(out, in_order(x_bank[LOOKUP_BANK[k]][:, 0:PAIR]),
                               ACT.Copy).then_inc(lookup_copied, 1)

            def stage_lookup(s, k):
                copy_lookup(s, k, in_order(looked_up[:, k, :]))

            def step(s, first, last):
                copy_transposes(s, 0)
                if not first:
                    relu1(s - 1, range(1))
                copy_blocks(s, 0, first)
                if not first:
                    relu1(s - 1, range(1, M1))
                if not last:
                    stage_lookup(s + 1, 0)
                if last:
                    copy_transposes(s, 1, range(2))
                    relu2(s - 1, range(1))
                    copy_transposes(s, 1, range(2, 3))
                    relu2(s - 1, range(1, M2))
                    copy_transposes(s, 1, range(3, NGRP))
                    copy_y(s - 1)
                if first:
                    stage_lookup(1, 1)
                if not last:
                    copy_transposes(s, 1)
                if not (first or last):
                    stage_lookup(s + 1, 1)
                if not (first or last):
                    relu2(s - 1)
                if not last:
                    stage_lookup(s + 1, 2)
                if not (first or last):
                    copy_y(s - 1)
                copy_blocks(s, 1, first)
                if not last:
                    act.wait_ge(gram_done, 2 * GBANKS * (s + 1))
                    act.wait_ge(lookup_copied, K1H * (s + 1) + STAGED)
                    for k in range(STAGED):
                        act.activation(slot(1 + NGATHER + k), in_order(looked_up[:, k, :]),
                                       ACT.Copy).then_inc(lookup_placed, 1)
                    place_dense(s + 1)
                    for k in range(STAGED, K1H):
                        copy_lookup(s + 1, k, slot(1 + NGATHER + k))

            for k in range(K1H):
                copy_lookup(0, k, slot(1 + NGATHER + k))
            round_row_table()
            act.wait_ge(dense_loaded, 16)
            place_dense(0)
            act.wait_ge(tail_weights_loaded, 64)
            over_pairs(act, step)
            def copy_y_tile(u):
                act.wait_ge(y_summed, PAIRS + u)
                act.wait_ge(y_stored, 16 * PAIRS)
                act.activation(y_tiles(u, u + 1), unit_cols(y_bank[u]), ACT.Copy).then_inc(y_copied, 1)

            relu1(PAIRS - 1, range(M1), TILE, h1_bank[0])
            relu2(PAIRS - 1, range(M2), TILE, h2_bank)
            relu1(PAIRS, range(M1), TILE, h1_bank[1])
            copy_y_tile(0)
            relu2(PAIRS, range(M2), TILE, h2_bank)
            copy_y_tile(1)

        @block.tensor
        def _(pe):
            def look_up_rows(s):
                pe.wait_ge(row_onehot_made, s)
                pe.wait_ge(transpose_copied, 2 * NGRP * s - NGRP + ROW_BANK + 1)
                for kt in range(RT):
                    last_mm = pe.matmul(row_parts, row_onehot[0:KROWS, kt, :], row_table[0:KROWS, kt, :, :],
                                        start=kt == 0, stop=kt == RT - 1)
                last_mm.then_inc(row_looked_up, 1)

            def look_up(s, k, first):
                pe.wait_ge(onehot_made, K1H * s + k + 1)
                if first:
                    pe.wait_ge(table_split, k + 1)
                for kt in range(KT):
                    for part, table in enumerate((table_hi, table_lo)):
                        last_mm = pe.matmul(x_bank[LOOKUP_BANK[k]][:, 0:PAIR], table[0:KROWS, k, kt, :],
                                            onehot[0:KROWS, k % 3, kt, :],
                                            start=kt + part == 0, stop=kt + part == KT)
                last_mm.then_inc(lookup_done, 1)

            def transpose_rows(s, u, first, groups=range(NGRP)):
                for g in groups:
                    if g == ROW_BANK and u == 0 and not first:
                        pe.wait_ge(row_placed, s)
                    if g == NGRP - 1 and u == 0:
                        pe.wait_ge(gathered[u][g], 16 * GRP + 16 * (GRP - 1) * s)
                    else:
                        pe.wait_ge(gathered[u][g], 16 * GRP * (s + 1))
                    if g >= TBANKS:
                        pe.wait_ge(transpose_copied, 2 * NGRP * s + NGRP * u + g - TBANKS + 1)
                    for i in range(GRP):
                        last_mm = pe.transpose(t_bank[g % TBANKS][:, i, :], rows[u][:, GRP * g + i, :], ident[:, :])
                    last_mm.then_inc(transposed, 1)

            def multiply_features(s, u, first):
                pe.wait_ge(transpose_copied, NGRP * (2 * s + u + 1))
                pe.wait_ge(lookup_copied, K1H * (s + 1))
                if not first:
                    pe.wait_ge(lookup_placed, STAGED * s)
                pe.wait_ge(dense_placed, s + 1)
                for i in range(GBANKS):
                    n = GBANKS * u + i
                    if not (first and n < 2):
                        pe.wait_ge(gram_copied[0], 2 * GBANKS * s + n - 1)
                        pe.wait_ge(gram_copied[1], 2 * GBANKS * s + n - 1)
                    for t in range(GRAMS_PER_BANK):
                        p = J * (GRAMS_PER_BANK * i + t)
                        last_mm = pe.matmul(
                            g_bank[i % 2][0:GRAM_ROWS, GRAM_COLS * t:GRAM_COLS * (t + 1)],
                            features[:, u, p:p + J, :].rearrange("d j f -> d (j f)")[:, 0:GRAM_ROWS],
                            features[:, u, p:p + J, 1:FEATURES], start=True, stop=True)
                    last_mm.then_inc(gram_done, 1)

            def h1_sum(m, u):
                return x_bank[m % 2][:, 0:PAIR] if u is None else h1_bank[u][m % 2][:, 0:TILE]

            def layer1_dense(n, m, u=None):
                if m >= 2:
                    pe.wait_ge(h1_ready, M1 * n + m - 1)
                if u is None:
                    pair, begin, end = dense[:, bass.ds(n * PAIR, PAIR)], 0, 2
                else:
                    pair, begin, end = dense[:, BATCH - PAIR:BATCH], u, u + 1
                x = pair.rearrange("d (j u t) -> d u j t", j=J, u=2)[:, begin:end, :, :]
                pe.matmul(h1_sum(m, u), w1d[:, 128 * m:128 * (m + 1)], x, start=True, stop=False)

            def layer1_interactions(n, m, u=None):
                begin, end = (0, 2) if u is None else (u, u + 1)
                if m == 0:
                    if u is None:
                        pe.wait_ge(z_shifted, 16 * SHIFTS * (n + 1))
                    else:
                        pe.wait_ge(z_half_shifted[u], 16 * (SHIFTS - u * POOL_SHIFTS))
                    if u == 1:
                        pe.wait_ge(z_half_shifted_by_pool, 16 * POOL_SHIFTS)
                for r in range(RTILES):
                    last_mm = pe.matmul(h1_sum(m, u), w1z[0:ZROWS, r, 128 * m:128 * (m + 1)],
                                        z[0:ZROWS, begin:end, :, r, :], start=False, stop=r == RTILES - 1)
                last_mm.then_inc(h1_summed, 1)

            def layer1(n, quarters, u=None):
                for m in quarters:
                    if m >= 2:
                        layer1_dense(n, m, u)
                    layer1_interactions(n, m, u)

            def layer2(n, m, width=PAIR, bank=x_bank):
                for k in range(M1):
                    if m == 0:
                        pe.wait_ge(h1_ready, M1 * n + max(k + 1, M1 - 1))
                    last_mm = pe.matmul(bank[m][:, 0:width], w2s[:, k, 128 * m:128 * (m + 1)],
                                        hidden1[:, k, 0:width], start=k == 0, stop=k == M1 - 1)
                last_mm.then_inc(h2_summed, 1)

            def layer3(n, width=PAIR, out=None):
                if out is None:
                    out = x_bank[1][0:1, 0:width]
                    pe.wait_ge(h2_ready, M2 * (n + 1))
                for k in range(M2):
                    pe.wait_ge(h2_ready, M2 * n + k + 1)
                    last_mm = pe.matmul(out, w3s[:, k:k + 1], hidden2[:, k, 0:width],
                                        start=k == 0, stop=k == M2 - 1)
                last_mm.then_inc(y_summed, 1)

            def step(s, first, last):
                transpose_rows(s, 0, first)
                if not first:
                    pe.wait_ge(lookup_copied, K1H * (s + 1))
                    for m in range(2):
                        layer1_dense(s - 1, m)
                    layer1(s - 1, range(1))
                multiply_features(s, 0, first)
                if not first:
                    layer1(s - 1, range(1, M1))
                if not last:
                    if not first:
                        pe.wait_ge(h1_ready, M1 * s - 1)
                    look_up(s + 1, 0, False)
                if last:
                    transpose_rows(s, 1, first, range(2))
                    layer2(s - 1, 0)
                    transpose_rows(s, 1, first, range(2, 3))
                    layer2(s - 1, 1)
                    transpose_rows(s, 1, first, range(3, NGRP))
                    layer3(s - 1)
                    multiply_features(s, 1, first)
                    return
                if first:
                    look_up(1, 1, False)
                transpose_rows(s, 1, first)
                if not first:
                    pe.wait_ge(h1_ready, M1 * s)
                    look_up(s + 1, 1, False)
                if first:
                    pe.wait_ge(row_table_split, len(row_raw))
                look_up_rows(s + 1)
                pe.wait_ge(lookup_copied, K1H * (s + 1) + 1)
                if not first:
                    layer2(s - 1, 0)
                    pe.wait_ge(lookup_copied, K1H * (s + 1) + 2)
                    layer2(s - 1, 1)
                    pe.wait_ge(h2_ready, M2 * s - 1)
                look_up(s + 1, 2, False)
                if not first:
                    layer3(s - 1)
                multiply_features(s, 1, first)
                pe.wait_ge(lookup_copied, K1H * (s + 1) + 3)
                look_up(s + 1, 3, False)
                if first:
                    pe.wait_ge(lookup_copied, K1H * (s + 1) + 2)
                else:
                    pe.wait_ge(y_copied, s)
                look_up(s + 1, 4, False)
                pe.wait_ge(lookup_copied, K1H * (s + 1) + 4)
                look_up(s + 1, 5, False)
                if first:
                    pe.wait_ge(w1z_loaded, 16)
                    pe.wait_ge(w1d_ready, 1)
                    pe.wait_ge(tail_weights_loaded, 64)

            for k in range(K1H):
                if k >= 2:
                    pe.wait_ge(lookup_copied, k)
                look_up(0, k, True)
            pe.wait_ge(ident_loaded, 16)
            pe.wait_ge(cleared, 2)
            over_pairs(pe, step)
            for u in range(2):
                if u == 0:
                    pe.wait_ge(y_copied, PAIRS - 1)
                else:
                    pe.wait_ge(gram_copied[0], 2 * GBANKS * PAIRS)
                    pe.wait_ge(gram_copied[1], 2 * GBANKS * PAIRS)
                for m in range(2):
                    layer1_dense(PAIRS - 1 + u, m, u)
                layer1(PAIRS - 1 + u, range(M1), u)
                if u == 1:
                    layer3(PAIRS - 1, TILE, y_bank[0])
                for m in range(M2):
                    layer2(PAIRS - 1 + u, m, TILE, h2_bank)
            layer3(PAIRS, TILE, y_bank[1])


def pair_weight_rows():
    feature = (0,) + tuple(f + 1 for f in GATHER_FIELDS) + tuple(f + 1 for f in ONEHOT_FIELDS)
    at = []
    for lo, hi in COLUMN_GROUPS:
        for left in range(hi):
            line = []
            for right in range(lo, lo + RTILES):
                if left < right <= hi:
                    a, b = sorted((feature[left], feature[right]))
                    line.append(D + a * (2 * FEATURES - a - 1) // 2 + b - a - 1)
                else:
                    line.append(-1)
            at.append(line)
    return at


def kernel(**inputs):
    import numpy as np
    import concourse.bacc as bacc
    from concourse.bass_utils import run_bass_kernel_spmd

    ids = np.asarray(inputs["ids"])
    w1 = np.asarray(inputs["W_top1"])
    at = np.array(pair_weight_rows())
    w_pairs = np.zeros((ZROWS, RTILES, H1), w1.dtype)
    w_pairs[at >= 0] = w1[at[at >= 0]]
    by_tile = ids.reshape(PAIRS, J, 2, GROUPS, FIELDS).transpose(0, 2, 3, 1, 4)
    arrays = {
        "ids_gather": by_tile[..., list(GATHER_FIELDS)].reshape(2 * PAIRS, TILE, NGATHER),
        "ids_onehot": np.concatenate([
            ids[:, list(ONEHOT_FIELDS)].reshape(PAIRS, PAIR, K1H).transpose(0, 2, 1).reshape(PAIRS, K1H * PAIR),
            by_tile[:, 0, :, :, ROW_FIELD].reshape(PAIRS, TILE)], axis=1),
        "dense_t": np.asarray(inputs["r_dense_output"]).T,
        "identity": np.eye(128, dtype=np.float32),
        "row_index": np.concatenate([np.arange(KROWS * kt, dtype=np.int32).reshape(KROWS, kt)
                                     for kt in (KT, RT)], axis=1),
        "w_pairs": w_pairs,
        "w_dense": np.stack([w1[:D], w1[-D:]]),
        "b1": np.asarray(inputs["b_top1"]).reshape(M1, 128).T,
        "w2": np.asarray(inputs["W_top2"]),
        "b2": np.asarray(inputs["b_top2"]).reshape(M2, 128).T,
        "w3": np.asarray(inputs["W_top3"]).reshape(M2, 128).T,
    }
    arrays |= {f"tbl_{f}": np.asarray(inputs[f"tbl_{f}"]) for f in range(FIELDS)}
    arrays = {name: np.ascontiguousarray(a) for name, a in arrays.items()}

    nc = bacc.Bacc("TRN2", target_bir_lowering=False, num_devices=1)
    ap = {name: nc.dram_tensor(name, a.shape, mybir.dt.from_np(a.dtype), kind="ExternalInput").ap()
          for name, a in arrays.items()}
    y = nc.dram_tensor("y", (BATCH, 1), mybir.dt.float32, kind="ExternalOutput").ap()
    build(nc, ap["ids_gather"], ap["ids_onehot"], ap["dense_t"], [ap[f"tbl_{f}"] for f in range(FIELDS)],
          ap["identity"], ap["row_index"], ap["w_pairs"], ap["w_dense"], ap["b1"], ap["w2"],
          ap["b2"], ap["w3"], y)
    return run_bass_kernel_spmd(nc, [arrays], core_ids=[0]).results[0]["y"]
```
